# Optimizing a Trainium2 kernel written in Bass

```python
import numpy as np
import jax
import jax.numpy as jnp

def _softmax(x, axis=-1):
    return jax.nn.softmax(x, axis=axis)

def _gelu(x):
    return jax.nn.gelu(x, approximate=True)

def _silu(x):
    return jax.nn.silu(x)

def _sigmoid(x):
    return jax.nn.sigmoid(x)

def _layernorm(x, axis=-1, eps=1e-05):
    m = jnp.mean(x, axis=axis, keepdims=True)
    v = jnp.var(x, axis=axis, keepdims=True)
    return (x - m) / jnp.sqrt(v + eps)

def _scatter_add(tgt, idx, src, axis=0):
    return tgt.at[idx].add(src)

def _segment_sum(src, seg, n):
    return jax.ops.segment_sum(src, seg, n)
kernel_name = 'mk_recurrent_d1_jaxref_r8_ba07e0'

def setup_inputs(seed: int=0):
    np.random.seed(seed)
    _w = jnp.asarray

    def _L0_attn_setup():
        import jax, jax.numpy as jnp
        import numpy as np
        HIDDEN = 512
        HEAD_DIM = 128
        N_Q_HEADS = 32
        N_KV_HEADS = 8
        SLIDING_WINDOW = 128
        ROPE_THETA = 10000.0
        BATCH, SEQ = (1, 256)

        def _rope(t, pos):
            d = t.shape[-1]
            half = d // 2
            inv_freq = ROPE_THETA ** (-jnp.arange(half, dtype=jnp.float32) / half)
            ang = pos[:, None].astype(jnp.float32) * inv_freq[None, :]
            cos = jnp.cos(ang)[None, :, None, :]
            sin = jnp.sin(ang)[None, :, None, :]
            t1, t2 = (t[..., :half], t[..., half:])
            return jnp.concatenate([t1 * cos - t2 * sin, t1 * sin + t2 * cos], axis=-1)
        key = jax.random.key(seed)
        ks = jax.random.split(key, 5)
        w_scale = HIDDEN ** (-0.5)
        return {'x': jax.random.normal(ks[0], (BATCH, SEQ, HIDDEN), jnp.float32), 'wq': jax.random.normal(ks[1], (HIDDEN, N_Q_HEADS * HEAD_DIM), jnp.float32) * w_scale, 'wk': jax.random.normal(ks[2], (HIDDEN, N_KV_HEADS * HEAD_DIM), jnp.float32) * w_scale, 'wv': jax.random.normal(ks[3], (HIDDEN, N_KV_HEADS * HEAD_DIM), jnp.float32) * w_scale, 'wo': jax.random.normal(ks[4], (N_Q_HEADS * HEAD_DIM, HIDDEN), jnp.float32) * w_scale}
    _L0_attn_in = _L0_attn_setup()

    def _L0_ffn_setup():
        import jax, jax.numpy as jnp
        import numpy as np
        import math
        SQRT7 = math.sqrt(7.0)
        EPS = 1e-05

        def int4_quant(x):
            beta = jnp.mean(jnp.abs(x), axis=-1, keepdims=True)
            x_q = jnp.clip(jnp.round(x * SQRT7 / (beta + EPS)), -8, 7)
            return x_q * (beta * SQRT7) / SQRT7

        def int8_quant(x):
            gamma = jnp.max(jnp.abs(x), axis=-1, keepdims=True)
            x_q = jnp.clip(jnp.round(x * 127.0 / (gamma + EPS)), -128, 127)
            return x_q * gamma / 127.0

        def bitlinear(x, w, scale):
            w_mean = jnp.mean(jnp.abs(w))
            w_q = jnp.clip(jnp.round(w / (w_mean + EPS)), -1.0, 1.0)
            w_eff = w_q * w_mean * scale
            return jnp.einsum('...i,oi->...o', x, w_eff)
        key = jax.random.key(seed)
        ks = jax.random.split(key, 4)
        H, I = (512, 1376)
        B, S = (2, 256)
        x = jax.random.normal(ks[0], (B, S, H), dtype=jnp.float32)
        w_gate = jax.random.uniform(ks[1], (I, H), jnp.float32, -1.0, 1.0) / np.sqrt(H)
        w_up = jax.random.uniform(ks[2], (I, H), jnp.float32, -1.0, 1.0) / np.sqrt(H)
        w_down = jax.random.uniform(ks[3], (H, I), jnp.float32, -1.0, 1.0) / np.sqrt(I)
        ones = jnp.ones((1,), jnp.float32)
        return {'x': x, 'w_gate': w_gate, 'w_up': w_up, 'w_down': w_down, 's_gate': ones, 's_up': ones, 's_down': ones}
    _L0_ffn_in = _L0_ffn_setup()
    _d = {'L0_attn_x': _L0_attn_in['x'], 'L0_attn_wq': _L0_attn_in['wq'], 'L0_attn_wk': _L0_attn_in['wk'], 'L0_attn_wv': _L0_attn_in['wv'], 'L0_attn_wo': _L0_attn_in['wo'], 'L0_ffn_w_gate': _L0_ffn_in['w_gate'], 'L0_ffn_w_up': _L0_ffn_in['w_up'], 'L0_ffn_w_down': _L0_ffn_in['w_down'], 'L0_ffn_s_gate': _L0_ffn_in['s_gate'], 'L0_ffn_s_up': _L0_ffn_in['s_up'], 'L0_ffn_s_down': _L0_ffn_in['s_down']}
    _x0 = _d['L0_attn_x']
    _d['L0_attn_x'] = jax.random.normal(jax.random.fold_in(jax.random.key(seed), 1), (2, 1024, 512), dtype=_x0.dtype)
    del _x0
    return _d

def reference(L0_attn_x, L0_attn_wq, L0_attn_wk, L0_attn_wv, L0_attn_wo, L0_ffn_w_gate, L0_ffn_w_up, L0_ffn_w_down, L0_ffn_s_gate, L0_ffn_s_up, L0_ffn_s_down):

    def _L0_attn_ref(x, wq, wk, wv, wo):
        import jax, jax.numpy as jnp
        import numpy as np
        HIDDEN = 512
        HEAD_DIM = 128
        N_Q_HEADS = 32
        N_KV_HEADS = 8
        SLIDING_WINDOW = 128
        ROPE_THETA = 10000.0
        BATCH, SEQ = (1, 256)

        def _rope(t, pos):
            d = t.shape[-1]
            half = d // 2
            inv_freq = ROPE_THETA ** (-jnp.arange(half, dtype=jnp.float32) / half)
            ang = pos[:, None].astype(jnp.float32) * inv_freq[None, :]
            cos = jnp.cos(ang)[None, :, None, :]
            sin = jnp.sin(ang)[None, :, None, :]
            t1, t2 = (t[..., :half], t[..., half:])
            return jnp.concatenate([t1 * cos - t2 * sin, t1 * sin + t2 * cos], axis=-1)
        B, S, _ = x.shape
        G = N_Q_HEADS // N_KV_HEADS
        sm_scale = HEAD_DIM ** (-0.5)
        q = (x @ wq).reshape(B, S, N_Q_HEADS, HEAD_DIM)
        k = (x @ wk).reshape(B, S, N_KV_HEADS, HEAD_DIM)
        v = (x @ wv).reshape(B, S, N_KV_HEADS, HEAD_DIM)
        pos = jnp.arange(S)
        q = _rope(q, pos)
        k = _rope(k, pos)
        qg = q.reshape(B, S, N_KV_HEADS, G, HEAD_DIM)
        scores = jnp.einsum('bqhgd,bshd->bhgqs', qg, k) * sm_scale
        i = pos[:, None]
        j = pos[None, :]
        allowed = (j <= i) & (j > i - SLIDING_WINDOW)
        neg = jnp.finfo(scores.dtype).min
        scores = jnp.where(allowed[None, None, None], scores, neg)
        attn = jax.nn.softmax(scores, axis=-1)
        out = jnp.einsum('bhgqs,bshd->bqhgd', attn, v).reshape(B, S, N_Q_HEADS * HEAD_DIM)
        return out @ wo

    def _L0_ffn_ref(x, w_gate, w_up, w_down, s_gate, s_up, s_down):
        import jax, jax.numpy as jnp
        import numpy as np
        import math
        SQRT7 = math.sqrt(7.0)
        EPS = 1e-05

        def int4_quant(x):
            beta = jnp.mean(jnp.abs(x), axis=-1, keepdims=True)
            x_q = jnp.clip(jnp.round(x * SQRT7 / (beta + EPS)), -8, 7)
            return x_q * (beta * SQRT7) / SQRT7

        def int8_quant(x):
            gamma = jnp.max(jnp.abs(x), axis=-1, keepdims=True)
            x_q = jnp.clip(jnp.round(x * 127.0 / (gamma + EPS)), -128, 127)
            return x_q * gamma / 127.0

        def bitlinear(x, w, scale):
            w_mean = jnp.mean(jnp.abs(w))
            w_q = jnp.clip(jnp.round(w / (w_mean + EPS)), -1.0, 1.0)
            w_eff = w_q * w_mean * scale
            return jnp.einsum('...i,oi->...o', x, w_eff)
        xq = int4_quant(x)
        gate = bitlinear(xq, w_gate, s_gate)
        up = bitlinear(xq, w_up, s_up)
        gate = jnp.square(jax.nn.relu(gate))
        inter = int8_quant(up * gate)
        return bitlinear(inter, w_down, s_down)
    x = L0_attn_x
    xn = _layernorm(x, axis=-1)
    s = _L0_attn_ref(xn, L0_attn_wq, L0_attn_wk, L0_attn_wv, L0_attn_wo)
    g = _silu(_L0_ffn_ref(xn, L0_ffn_w_gate, L0_ffn_w_up, L0_ffn_w_down, L0_ffn_s_gate, L0_ffn_s_up, L0_ffn_s_down))
    x = x + s * g
    return x

_drawn_inputs = setup_inputs


def setup_inputs(seed=0):
    import zlib

    import numpy as np

    out = dict(_drawn_inputs(seed))
    spreads = {}
    factors = {}
    for name, (base, spread) in spreads.items():
        noise = np.random.default_rng([zlib.crc32(name.encode()), seed]).standard_normal(out[name].shape)
        drawn = base * np.exp(spread * noise) if base else spread * noise
        out[name] = jnp.asarray(drawn.astype(out[name].dtype))
    for name, factor in factors.items():
        out[name] = (out[name] * factor).astype(out[name].dtype)
    return out
```

```python
import math

import concourse.bass as bass
from concourse import mybir
from concourse.alu_op_type import AluOpType as ALU

F32 = mybir.dt.float32
F32R = mybir.dt.float32r
BF16 = mybir.dt.bfloat16
U32 = mybir.dt.uint32
ACT = mybir.ActivationFunctionType
AX = mybir.AxisListType

P = 128
BATCH, SEQ, HID = 2, 1024, 512
HEADS, KV_HEADS, HD = 32, 8, 128
GROUP = HEADS // KV_HEADS
INTER = 1376
KT = HID // P
TILES = BATCH * SEQ // P
TPB = SEQ // P
BLK = 512
TPK = BLK // P
IT = (INTER + P - 1) // P
IPAD = IT * P
IREST = INTER - (IT - 1) * P
CHUNKS = [(0, 512), (512, 512), (1024, IPAD - 1024)]
NC = len(CHUNKS)
EPS = 1e-5
SQRT7 = math.sqrt(7.0)
ROUND_PARTS = [(0, 6 * HID), (6 * HID, IT * HID)]
MAGIC = 1.5 * 2.0**23
NEG = -3.0e38
ITERS = BATCH * KV_HEADS
PIECES = GROUP + GROUP + 2


def wait(eng, sem, value):
    if isinstance(value, int) and value <= 0:
        return
    eng.wait_ge(sem, value)


class Arena:

    def __init__(self, nc):
        self.nc, self.at = nc, (nc.sbuf_base + 63) // 64 * 64

    def tensor(self, name, shape, dtype):
        size = 2 if dtype == BF16 else 4
        for n in shape[1:]:
            size *= n
        t = self.nc.alloc_sbuf_tensor_at(name, shape, dtype, offset=self.at)
        self.at += (size + 31) // 32 * 32
        assert self.at <= self.nc.sbuf_usable_end, (name, self.at)
        return t


class Prepared:

    PARTS = 4

    def __init__(self, nc, arena):
        sem = nc.alloc_semaphore
        self.raw = [arena.tensor(f"w_raw{m}", [P, IT * HID], F32) for m in range(3)]
        self.ones = arena.tensor("ones", [P, P], F32)
        self.abs = arena.tensor("w_abs", [P, 3, self.PARTS], F32)
        self.mean = arena.tensor("w_mean", [P, 3], F32)
        self.inv = arena.tensor("w_inv", [P, 3], F32)
        self.scale = arena.tensor("w_scale", [P, 3], F32)
        self.s_in = arena.tensor("s_in", [P, 3], F32)
        self.s_fetch = [sem(f"s_fetch{m}") for m in range(3)]
        self.fetched = (32, 32, 16)
        self.s_scale, self.s_pad, self.s_ones, self.s_wsum, self.s_winv, self.s_wlink = (
            sem(n) for n in ("s_scale", "s_pad", "s_ones", "s_wsum", "s_winv", "s_wlink"))
        self.s_wabs = [sem(f"s_wabs{m}") for m in range(3)]
        self.s_wscaled = [sem(f"s_wscaled{m}") for m in range(3)]
        self.links = 0

    def part(self, m, i):
        n = IT * HID // self.PARTS
        return self.raw[m][:, i * n:(i + 1) * n]

    def ready(self, eng, m):
        eng.wait_ge(self.s_fetch[m], self.fetched[m])
        eng.wait_ge(self.s_pad, 3)

    def pad(self, dve):
        dve.memset(self.ones[:, :], 1.0).then_inc(self.s_ones, 1)
        for m in range(2):
            dve.memset(self.raw[m][IREST:P, (IT - 1) * HID:IT * HID], 0.0).then_inc(self.s_pad, 1)
        dve.memset(self.raw[2][:, :].rearrange("p (t n) -> p t n", n=IPAD)[:, :, INTER:IPAD], 0.0).then_inc(self.s_pad, 1)

    def sum_abs_act(self, act, m, i, unused):
        self.ready(act, m)
        act.activation(unused, self.part(m, i), ACT.Abs, accum_out=self.abs[:, m, i:i + 1]).then_inc(self.s_wabs[m], 1)
        act.wait_ge(self.s_wabs[m], i + 1)

    def sum_abs_dve(self, dve, m, i):
        self.ready(dve, m)
        dve.tensor_reduce(self.abs[:, m, i:i + 1], self.part(m, i), AX.X, ALU.add,
                          apply_absolute_value=True).then_inc(self.s_wabs[m], 1)

    def total(self, pe, m, bank):
        pe.wait_ge(self.s_ones, 1)
        pe.wait_ge(self.s_wabs[m], self.PARTS)
        pe.matmul(bank[:, 0:self.PARTS], self.ones[:, :], self.abs[:, m, :], start=True, stop=True).then_inc(self.s_wsum, 1)

    def scales(self, dve, m, bank):
        def link(ins):
            self.links += 1
            ins.then_inc(self.s_wlink, 1)
            dve.wait_ge(self.s_wlink, self.links)

        at = slice(m, m + 1)
        dve.wait_ge(self.s_wsum, m + 1)
        link(dve.tensor_reduce(self.mean[:, at], bank[:, 0:self.PARTS], AX.X, ALU.add))
        link(dve.tensor_scalar(self.mean[:, at], self.mean[:, at], 1.0 / (INTER * HID), None, ALU.mult))
        link(dve.tensor_scalar(self.inv[:, at], self.mean[:, at], EPS, None, ALU.add))
        dve.reciprocal(self.inv[:, at], self.inv[:, at]).then_inc(self.s_winv, 1)
        dve.wait_ge(self.s_scale, 48)
        link(dve.tensor_tensor(self.scale[:, at], self.mean[:, at], self.s_in[:, at], ALU.mult))

    def round(self, eng, m):
        eng.wait_ge(self.s_winv, m + 1)
        self.ready(eng, m)
        eng.wait_ge(self.s_wabs[m], self.PARTS)
        for a, b in ROUND_PARTS:
            part = self.raw[m][:, a:b]
            eng.tensor_scalar(part, part, self.inv[:, m:m + 1], MAGIC, ALU.mult, ALU.add).then_inc(self.s_wscaled[m], 1)


def build_kernel(nc, x, wq, wk, wv, wo, w_gate, w_up, w_down, scale_gate, scale_up, scale_down, rope, masks, out):
    arena = Arena(nc)
    banks = [nc.alloc_psum_tensor(f"bank{i}", [P, 512], F32) for i in range(8)]
    const = arena.tensor("const", [P, 4, P], F32)
    beta = arena.tensor("beta", [P, TILES], F32)
    start = arena.at
    q4_dram = nc.dram_tensor("int4_scratch", [BATCH * SEQ, HID], BF16, kind="Internal").ap()
    s_dram = nc.dram_tensor("attention_scratch", [BATCH * SEQ, HID], F32, kind="Internal").ap()
    weights = Prepared(nc, arena)
    ffn_at = arena.at
    s_store = [nc.alloc_semaphore(f"s_store{j}") for j in range(TPB)]
    arena.at = start
    attention(nc, arena, banks, x, wq, wk, wv, wo, w_gate, w_up, w_down, scale_gate, scale_up, scale_down, rope, masks,
              const, beta, weights, s_store, q4_dram, s_dram)
    arena.at = ffn_at
    ffn(nc, arena, banks, x, const, beta, weights, s_store, q4_dram, s_dram, out)


def attention(nc, arena, banks, x, wq, wk, wv, wo, w_gate, w_up, w_down, scale_gate, scale_up, scale_down, rope, masks,
              const, beta, weights, s_store, q4_dram, s_dram):
    sem = nc.alloc_semaphore
    ident, on_or_before, after, after_t = (const[:, i, :] for i in range(4))
    QK = GROUP + 1
    xn_at = arena.at
    xn_hi = arena.tensor("xn_hi", [P, BATCH, KT, SEQ], F32R)
    xn_lo = arena.tensor("xn_lo", [P, BATCH, KT, SEQ], F32R)
    row_bytes = KT * SEQ * 4
    w_hi = arena.tensor("w_hi", [P, GROUP + 2, KT, HD], F32R)
    w_lo = arena.tensor("w_lo", [P, GROUP + 2, KT, HD], F32R)
    wo_hi = arena.tensor("wo_hi", [P, GROUP, HID], F32R)
    wo_lo = arena.tensor("wo_lo", [P, GROUP, HID], F32R)
    raw = arena.tensor("raw", [P, GROUP, HID], F32)
    acc = arena.tensor("acc", [P, TPB, HID], F32)
    q_hi = arena.tensor("q_hi", [P, GROUP, 3, BLK // 2], F32R)
    q_lo = arena.tensor("q_lo", [P, GROUP, 3, BLK // 2], F32R)
    k_hi = arena.tensor("k_hi", [P, SEQ], F32R)
    k_lo = arena.tensor("k_lo", [P, SEQ], F32R)
    v_t = arena.tensor("v_t", [P, BLK], F32)
    v_hi = arena.tensor("v_hi", [P, TPB, HD], F32R)
    v_lo = arena.tensor("v_lo", [P, TPB, HD], F32R)
    prob = arena.tensor("prob", [P, 2, GROUP, P], F32)
    pt_at = arena.at
    pt = arena.tensor("pt", [P, 2, GROUP, P], F32)
    arena.at = pt_at
    pt_lo = arena.tensor("pt_lo", [P, 2, GROUP, P], F32R)
    pt_hi = arena.tensor("pt_hi", [P, 2, GROUP, P], F32R)
    o_hi = arena.tensor("o_hi", [P, GROUP, P], F32R)
    o_lo = arena.tensor("o_lo", [P, GROUP, P], F32R)
    rot_a = arena.tensor("rot_a", [P, 2, BLK], F32)
    rot_b_at = arena.at
    rot_b = arena.tensor("rot_b", [P, 2, BLK], F32)
    cos_sin = arena.tensor("cos_sin", [P, 2, SEQ], F32)
    neg = arena.tensor("neg", [P, 1], F32)
    negmax = arena.tensor("negmax", [P, 2, GROUP], F32)
    rowsum = arena.tensor("rowsum", [P, 2, GROUP], F32)
    rinv = arena.tensor("rinv", [P, 2, GROUP], F32)
    stats = arena.tensor("stats", [P, TPB, 6], F32)
    mv = arena.tensor("mv", [P, TILES, 2], F32)
    rstd = arena.tensor("rstd", [P, TILES], F32)
    rs = arena.tensor("rs", [P, 3, TPB], F32)
    xt = arena.tensor("xt", [P, HID], F32)
    qz = arena.tensor("qz", [P, HID], BF16)
    abs_sum = arena.tensor("abs_sum", [P, 1], F32)
    xk = arena.tensor("xk", [P, 1], F32)
    end = arena.at
    x_rows = []
    for b, at in enumerate((xn_at + 3 * row_bytes, xn_at + row_bytes)):
        arena.at = at
        x_rows.append(arena.tensor(f"x_rows{b}", [P, TPB, HID], F32))
    arena.at = rot_b_at
    unused = arena.tensor("unused_abs", [P, IT * HID // weights.PARTS], BF16)
    arena.at = end

    bank_s = [banks[0], banks[1]]
    bank_pt, bank_pv, bank_wo, bank_vt = banks[2], banks[3], banks[4], banks[5]
    bank_chunk = [banks[6], banks[7]]

    s_masks, s_rope, s_neg, s_step = (sem(n) for n in ("s_masks", "s_rope", "s_neg", "s_step"))
    s_rows = [None] + [sem(f"s_rows{g}") for g in range(1, TILES // TPK)]
    s_row = [sem(f"s_row{t}") for t in range(TPK)]
    s_bn, s_var, s_root, s_xn, s_xtr, s_xhi, s_xlo = (
        sem(n) for n in ("s_bn", "s_var", "s_root", "s_xn", "s_xtr", "s_xhi", "s_xlo"))
    s_xt, s_abs, s_vq, s_qz, s_q4 = (sem(n) for n in ("s_xt", "s_abs", "s_vq", "s_qz", "s_q4"))
    s_wload = [sem(f"s_wload{i}") for i in range(GROUP)]
    s_whi, s_wlo, s_wlo2 = sem("s_whi"), sem("s_wlo"), sem("s_wlo2")
    s_chunk, s_swap, s_rot_a, s_rot_b, s_rot, s_qkhi, s_qklo = (
        sem(n) for n in ("s_chunk", "s_swap", "s_rot_a", "s_rot_b", "s_rot", "s_qkhi", "s_qklo"))
    s_vcopy, s_vt, s_v, s_vlo = sem("s_vcopy"), sem("s_vt"), sem("s_v"), sem("s_vlo")
    s_pch, s_pph, s_pcl, s_ppl = sem("s_pch"), sem("s_pph"), sem("s_pcl"), sem("s_ppl")
    s_scores, s_cur, s_merged, s_negmax, s_pexp, s_rinv, s_prob = (
        sem(n) for n in ("s_scores", "s_cur", "s_merged", "s_negmax", "s_pexp", "s_rinv", "s_prob"))
    s_ptr, s_ptc, s_ptp, s_pv, s_ohi, s_olo, s_wo, s_acc = (
        sem(n) for n in ("s_ptr", "s_ptc", "s_ptp", "s_pv", "s_ohi", "s_olo", "s_wo", "s_acc"))

    def heads(t):
        return t.rearrange("p (h n) -> p h n", h=GROUP)

    def q_block(q, h, par):
        return q[:, h, 0:2 + par:1 + par, :]

    def q_tile(q, h, par, t):
        return q[:, h, 0 if t < 2 else 1 + par, (t % 2) * P:(t % 2 + 1) * P]

    def over_heads(m):
        return m.unsqueeze(1).to_broadcast([P, GROUP, P])

    def over_keys(v4):
        return v4.unsqueeze(2).to_broadcast([P, GROUP, P])

    NCH = GROUP + 2
    V = GROUP + 1

    def halves(s):
        order = [(c, h) for c in range(NCH) for h in range(2)]
        flat = [(2, *order[0])] + [(2, *o) for o in order[1:4]] + [(1, *o) for o in order[4:]]
        slots = {2: [None, None, flat[0]], 3: flat[1:4], 0: flat[4:7], 1: flat[7:10]}
        slots[2][0:2] = flat[10:12]
        return slots[s]

    def finished(s, place):
        ahead, c, h = halves(s)[place]
        return (ahead, c) if h == 1 else None

    def late(it, j, last_it):
        at = j - 1
        done = finished(at % TPK, 1 if at == 0 else 2)
        if done is None or (last_it and at // TPK + done[0] >= 2):
            return None
        return 2 * it + at // TPK + done[0], (at // TPK + done[0]) % 2, done[1]

    SPLIT_AT = {1: [0], 2: [1], 3: [2, 3], 4: [4], 5: [5]}
    OWN = PIECES - 2

    def loops(eng, body):
        body(0, False)
        with eng.Fori(1, ITERS - 1) as it:
            body(it, False)
        body(ITERS - 1, True)

    def wq_piece(kv, c):
        w, head = ((wk, kv), *[(wq, kv * GROUP + i) for i in range(GROUP)], (wv, kv))[c]
        return w.rearrange("(k p) n -> p k n", p=P)[:, :, bass.ds(head * HD, HD)]

    with nc.Block() as block:
        @block.sync
        def _(sp):
            def load_rows(g):
                b, t = g * TPK // TPB, g * TPK % TPB
                sp.dma_start(x_rows[b][:, t:t + TPK, :],
                             x[b, t * P:(t + TPK) * P, :].rearrange("(t p) n -> p t n", p=P)).then_inc(s_rows[g], 16)

            def load(ring, src, dst):
                sp.dma_start(dst, src).then_inc(s_wload[ring], 16)

            def load_chunk(kv, c):
                load(c % 2, wq_piece(kv, c), raw[:, c % 2, :].rearrange("p (k n) -> p k n", k=KT))

            for t in range(TPK):
                sp.dma_start(x_rows[0][:, t, :], x[0, t * P:(t + 1) * P, :]).then_inc(s_row[t], 16)
            sp.dma_start(const[:, :, :], masks).then_inc(s_masks, 16)
            for c in range(2):
                load_chunk(0, c)
            load_rows(1)
            sp.dma_start(cos_sin[:, :, :], rope).then_inc(s_rope, 16)
            for c in range(2, NCH):
                sp.wait_ge(s_wlo, c - 1)
                load_chunk(0, c)
            load_rows(2)
            load_rows(3)

            def body(it, last, stores=()):
                kv, kv_next = it % KV_HEADS, (it + 1) % KV_HEADS

                def load_wo(h, *before):
                    wait(sp, *before)
                    load(h, wo[bass.ds((kv * GROUP + h) * HD, HD), :], raw[:, h, :])

                load_wo(0, s_wlo, OWN * it + 5)
                load_wo(1, s_wlo, OWN * it + 6)
                for h in range(2, GROUP):
                    load_wo(h, s_wlo2, 2 * it if isinstance(it, int) else it * 2)
                for j in stores:
                    store(it // KV_HEADS - 1, j)
                sp.wait_ge(s_xtr, TPB + it)
                wait(sp, s_qz, it)
                row = (1 - it // KV_HEADS) * SEQ + (it % KV_HEADS) * P
                rows = x.rearrange("b t n -> (b t) n")
                sp.dma_start(xt[:, :], rows[bass.ds(row, P), :]).then_inc(s_xt, 16)
                if not last:
                    for c in range(NCH):
                        sp.wait_ge(s_wlo, NCH + OWN * it + c + 1)
                        load_chunk(kv_next, c)
                else:
                    fetch()
                store_q4(it, row)

            def fetch():
                sp.wait_ge(s_chunk, NCH * 2 * ITERS)
                sp.wait_ge(s_xlo, TPB + ITERS)
                for w, to, s in zip((w_gate, w_up), weights.raw, weights.s_fetch):
                    dst = to[:, :].rearrange("p (t n) -> p t n", n=HID)
                    sp.dma_start(dst[:, 0:IT - 1, :], w[0:(IT - 1) * P, :].rearrange("(t p) n -> p t n", p=P)).then_inc(s, 16)
                    sp.dma_start(dst[0:IREST, IT - 1, :], w[(IT - 1) * P:INTER, :]).then_inc(s, 16)
                for i, s in enumerate((scale_gate, scale_up, scale_down)):
                    sp.dma_start(weights.s_in[:, i:i + 1], s.unsqueeze(0).to_broadcast([P, 1])).then_inc(weights.s_scale, 16)
                sp.dma_start(weights.raw[2][:, :].rearrange("p (t n) -> p t n", n=IPAD)[:, :, 0:INTER],
                             w_down.rearrange("(t p) n -> p t n", p=P)).then_inc(weights.s_fetch[2], 16)

            def store_q4(it, row):
                sp.wait_ge(s_masks, 16)
                sp.wait_ge(s_qz, it + 1)
                sp.dma_start(q4_dram[bass.ds(row, P), :], qz[:, :]).then_inc(s_q4, 16)

            def store(b, j):
                sp.wait_ge(s_acc, TPB * (KV_HEADS * (b + 1) - 1) + j + 1)
                row = b * SEQ + j * P
                sp.dma_start(s_dram[row:row + P, :], acc[:, j, :]).then_inc(s_store[j], 16)

            body(0, False)
            with sp.Fori(1, KV_HEADS) as it:
                body(it, False)
            for j in range(TPB - 2):
                store(0, j)
            body(KV_HEADS, False, stores=(TPB - 2, TPB - 1))
            with sp.Fori(KV_HEADS + 1, ITERS - 1) as it:
                body(it, False)
            body(ITERS - 1, True)
            for j in range(TPB):
                store(1, j)
            sp.wait_ge(s_q4, 16 * ITERS)

        @block.tensor
        def _(pe):
            pe.wait_ge(s_masks, 16)

            def transpose_x(t, src, bank):
                for k in range(KT):
                    last = pe.transpose(bank[:, k * P:(k + 1) * P], src[:, k * P:(k + 1) * P], ident)
                last.then_inc(s_xtr, 1)

            def project(it, block, par, c, half):
                bank = bank_chunk[c % 2]
                n = NCH * block + c
                if half == 0:
                    if c in (0, 1):
                        before = c + GROUP
                        if before == V:
                            wait(pe, s_vcopy, block)
                        else:
                            wait(pe, s_rot_a, QK * block)
                    else:
                        wait(pe, s_rot_a, QK * block + c - 1)
                    wait(pe, s_wlo, OWN * it + c + 1)
                    if c == 0:
                        pe.wait_ge(s_xlo, TPK * (par + 1) if isinstance(it, int) and it == 0 else x_ready(it, par))
                batch = it // KV_HEADS
                cols = slice(par * BLK, (par + 1) * BLK)
                for k in range(2 * half, 2 * half + 2):
                    for i, (w, xn) in enumerate(((w_hi, xn_hi), (w_hi, xn_lo), (w_lo, xn_hi))):
                        rhs = xn[:, batch, k, cols] if isinstance(batch, int) else \
                            xn[:, bass.ds(batch, 1), k, cols].rearrange("p a n -> p (a n)")
                        last = pe.matmul(bank[:, :], w[:, c, k, :], rhs,
                                         start=(k == 0 and i == 0), stop=(k == KT - 1 and i == 2))
                if half == 1:
                    last.then_inc(s_chunk, 1)

            def x_ready(it, par):
                return TPB + it - 1 + par

            def transpose_v(block, tiles):
                wait(pe, s_vcopy, block + 1)
                wait(pe, s_vlo, block)
                pe.wait_ge(s_xlo, tiles)
                for i in range(TPK):
                    last = pe.transpose(bank_vt[:, i * P:(i + 1) * P], v_t[:, i * P:(i + 1) * P], ident)
                last.then_inc(s_vt, 1)

            def scores(tile, block, j):
                wait(pe, s_qklo, QK * (block + 1) - 1)
                wait(pe, s_merged, tile)
                j %= TPB
                first = j == 0
                keys = slice(j * P, (j + 1) * P) if first else slice((j - 1) * P, (j + 1) * P)
                n = P if first else 2 * P
                par, t = j // TPK % 2, j % TPK
                for h in range(GROUP):
                    if h == GROUP - 1:
                        wait(pe, s_qklo, QK * (block + 1))
                    dst = bank_s[h // 2][:, (h % 2) * 2 * P + 2 * P - n:(h % 2) * 2 * P + 2 * P]
                    for i, (q, k) in enumerate(((q_hi, k_hi), (q_hi, k_lo), (q_lo, k_hi))):
                        last = pe.matmul(dst, q_tile(q, h, par, t), k[:, keys], start=(i == 0), stop=(i == 2))
                last.then_inc(s_scores, 1)

            def transpose_p(tile, it, j):
                pe.wait_ge(s_prob, tile + 1)
                wait(pe, s_ptc, tile)
                wait(pe, s_ptp, (TPB - 1) * it + max(j - 1, 0))
                for h in range(GROUP):
                    last = pe.transpose(bank_pt[:, h * P:(h + 1) * P], prob[:, j % 2, h, :], ident)
                last.then_inc(s_ptr, 1)

            def body(it, last_it):
                def ahead(j):
                    return 0 < j < TPB

                for j in range(TPB):
                    tile, s = TPB * it + j, j % TPK
                    block = 2 * it + j // TPK

                    def piece(place):
                        ahead, c, half = halves(s)[place]
                        b = block + ahead
                        nxt = j // TPK + ahead
                        if nxt >= 2 and last_it:
                            return
                        project(it if nxt < 2 else it + 1, b, nxt % 2, c, half)

                    if not ahead(j):
                        transpose_p(tile, it, j)
                    piece(0)
                    piece(1)
                    if s == 3 and not (last_it and j == TPB - 1):
                        transpose_v(block + 1, TPB + it + 1)
                    pe.wait_ge(s_vlo, block + 1)
                    wait(pe, s_ohi, tile)
                    wait(pe, s_olo, tile)
                    for before in range(min(j, 1) + 1):
                        if before == 0:
                            pe.wait_ge(s_pcl, tile + 1)
                        else:
                            wait(pe, s_ppl, (TPB - 1) * it + j)
                        hi, lo = (a[:, before, :, :].rearrange("p h n -> p (h n)") for a in (pt_hi, pt_lo))
                        for i, (a, b) in enumerate(((v_hi, hi), (v_lo, hi), (v_hi, lo))):
                            last = pe.matmul(bank_pv[:, :], a[:, j - before, :], b, start=(before == 0 and i == 0),
                                             stop=(before == min(j, 1) and i == 2))
                    last.then_inc(s_pv, 1)
                    if not (last_it and j >= TPB - 2):
                        scores(tile + 2, 2 * it + (j + 2) // TPK, j + 2)
                    if j == 2:
                        pe.wait_ge(s_xn, TPB + it + 1)
                        pe.wait_ge(s_vlo, 2 * it + 1)
                        transpose_x(0, xt, bank_vt)
                    piece(2)
                    if last_it and j == TPB - 1:
                        wait(pe, s_rot_a, QK * 2 * ITERS)
                        weights.total(pe, 0, bank_chunk[0])
                    if ahead(j + 1):
                        transpose_p(tile + 1, it, j + 1)
                    pe.wait_ge(s_olo, tile + 1)
                    wait(pe, s_acc, tile)
                    order = (0, 2, 1, 3)
                    for h in order:
                        if j == 0 and h < 2:
                            pe.wait_ge(s_wlo, NCH + OWN * it + h + 1)
                        elif j == 0:
                            pe.wait_ge(s_wlo2, 2 * it + h - 1)
                        for i, (o, w) in enumerate(((o_hi, wo_hi), (o_hi, wo_lo), (o_lo, wo_hi))):
                            last = pe.matmul(bank_wo[:, :], o[:, h, :], w[:, h, :],
                                             start=(h == order[0] and i == 0), stop=(h == order[-1] and i == 2))
                    last.then_inc(s_wo, 1)

            for t in range(TPB):
                if t in (TPK, TPK + 2):
                    for half in range(2):
                        project(0, 0, 0, (t - TPK) // 2, half)
                pe.wait_ge(s_xn, t + 1)
                wait(pe, s_xlo, t - 3)
                transpose_x(t, x_rows[0][:, t, :], banks[t % 4])
            for c in range(2, NCH):
                for half in range(2):
                    project(0, 0, 0, c, half)
            for half in range(2):
                project(0, 1, 1, 0, half)
            pe.wait_ge(s_xlo, TPB)
            scores(0, 0, 0)
            transpose_v(0, TPB)
            scores(1, 0, 1)
            for half in range(2):
                project(0, 1, 1, 1, half)
            loops(pe, body)

        @block.scalar
        def _(act):
            def swap(block, par, c):
                r, slot = QK * block + c, (par + c) % 2
                act.wait_ge(s_chunk, NCH * block + c + 1)
                wait(act, s_rot, r - 1)
                half = HD // 2
                act.activation(rot_b[0:half, slot, :], bank_chunk[c % 2][half:P, :], ACT.Copy).then_inc(s_swap, 1)
                act.activation(rot_b[half:P, slot, :], bank_chunk[c % 2][0:half, :], ACT.Copy).then_inc(s_swap, 1)

            def high(block, par, c):
                r, slot = QK * block + c, (par + c) % 2
                act.wait_ge(s_rot, r + 1)
                if c == 0:
                    wait(act, s_scores, TPK * block - 3)
                    dst = k_hi[:, par * BLK:(par + 1) * BLK]
                else:
                    wait(act, s_scores, TPK * (block - 1) + 2)
                    dst = q_block(q_hi, c - 1, par)
                src = rot_a[:, slot, :]
                if c > 0:
                    src = src.rearrange("p (a n) -> p a n", a=2)
                act.activation(dst, src, ACT.Copy).then_inc(s_qkhi, 1)

            def copy_v(block):
                act.wait_ge(s_chunk, NCH * (block + 1))
                wait(act, s_vt, block)
                act.activation(v_t[:, :], bank_chunk[V % 2][:, :], ACT.Copy).then_inc(s_vcopy, 1)

            def place_v(block, par):
                wait(act, s_vt, block + 1)
                wait(act, s_pv, TPK * block - 3)
                act.activation(v_hi[:, par * TPK:(par + 1) * TPK, :],
                               bank_vt[:, :].rearrange("p (t n) -> p t n", n=HD), ACT.Copy).then_inc(s_v, 1)

            def root(g, n=TPK):
                act.wait_ge(s_var, g + 1)
                act.activation(rs[:, 1, 0:n], rs[:, 0, 0:n], ACT.Sqrt).then_inc(s_root, 1)

            def high_x(n, batch, tok, bank):
                act.wait_ge(s_xtr, n + 1)
                dst = xn_hi[:, batch, :, tok:tok + P] if isinstance(batch, int) and isinstance(tok, int) else \
                    xn_hi[:, bass.ds(batch, 1), :, bass.ds(tok, P)].rearrange("p a k n -> p (a k) n")
                act.activation(dst, bank[:, :].rearrange("p (k n) -> p k n", k=KT), ACT.Copy).then_inc(s_xhi, 1)

            def split(loads, ring, uses, dst):
                act.wait_ge(s_wload[ring], 16 * loads if isinstance(loads, int) else loads * 16)
                wait(act, *uses)
                act.activation(dst, raw[:, ring, :], ACT.Copy).then_inc(s_whi, 1)

            def copy_current(tile, j):
                act.wait_ge(s_scores, tile + 1)
                wait(act, s_ptr, tile - 1)
                for b in range(2):
                    src = bank_s[b][:, :].rearrange("p (h s n) -> p h s n", h=2, s=2)[:, :, 1, :]
                    act.activation(prob[:, j % 2, 2 * b:2 * b + 2, :], src, ACT.Copy).then_inc(s_cur, 1)

            def exponential(tile, j):
                act.wait_ge(s_negmax, tile + 1)
                wait(act, s_rinv, tile - 1)
                for h in range(GROUP):
                    last = act.activation(prob[:, j % 2, h, :], prob[:, j % 2, h, :], ACT.Exp,
                                          bias=negmax[:, j % 2, h:h + 1], accum_out=rowsum[:, j % 2, h:h + 1])
                last.then_inc(s_pexp, 1)

            def flat(w, c):
                return w[:, c, :, :].rearrange("p k n -> p (k n)")

            def sum_weights(m, parts):
                act.wait_ge(s_rot, QK * 2 * ITERS)
                for i in parts:
                    weights.sum_abs_act(act, m, i, unused[:, :])

            def high_o(tile):
                act.wait_ge(s_pv, tile + 1)
                wait(act, s_wo, tile)
                act.activation(o_hi[:, :, :], heads(bank_pv[:, :]), ACT.Copy).then_inc(s_ohi, 1)

            def body(it, last_it):
                for j in range(TPB):
                    tile, s = TPB * it + j, j % TPK
                    block = 2 * it + j // TPK

                    def chunk(place, step):
                        if finished(s, place) is None or (j == 0 and step == 1):
                            return
                        ahead, c = finished(s, place)
                        nxt = j // TPK + ahead
                        if nxt >= 2 and last_it:
                            return
                        if c == V:
                            if step == 0:
                                copy_v(block + ahead)
                        else:
                            (swap, high)[step](block + ahead, nxt % 2, c)

                    act.wait_ge(s_ptc, tile + 1)
                    wait(act, s_pv, tile)
                    act.activation(pt_hi[:, 0, :, :], pt[:, 0, :, :], ACT.Copy).then_inc(s_pch, 1)
                    if j > 0:
                        wait(act, s_ptp, (TPB - 1) * it + j)
                        act.activation(pt_hi[:, 1, :, :], pt[:, 1, :, :], ACT.Copy).then_inc(s_pph, 1)
                    if s == 2 and late(it, j, last_it):
                        high(*late(it, j, last_it))
                    if last_it and j == TPB - 1:
                        sum_weights(0, (2, 3))
                    else:
                        exponential(tile + 1, j + 1)
                    if j == 0:
                        high_o(tile)
                        for h in range(GROUP):
                            split((NCH + OWN * it) // 2 + 1 if h < 2 else it + 1, h, (s_wo, tile), wo_hi[:, h, :])
                    if s != 2 and late(it, j, last_it):
                        high(*late(it, j, last_it))
                    if j == 6:
                        act.wait_ge(s_vq, it + 1)
                        act.wait_ge(s_abs, it + 1)
                        act.activation(qz[:, :], xt[:, :], ACT.Copy, bias=-MAGIC).then_inc(s_qz, 1)
                    if j == 2:
                        act.wait_ge(s_xn, TPB + it + 1)
                        wait(act, s_q4, 16 * it if isinstance(it, int) else it * 16)
                        act.activation(qz[:, :], xt[:, :], ACT.Abs, accum_out=abs_sum[:, :]).then_inc(s_abs, 1)
                    chunk(0, 0)
                    chunk(1, 0)
                    if j > 0:
                        high_o(tile)
                    if last_it and j >= TPB - 2:
                        sum_weights(0 if j == TPB - 2 else 2, (0, 1) if j == TPB - 2 else range(weights.PARTS))
                    if s == 3 and not (last_it and j == TPB - 1):
                        place_v(block + 1, (j // TPK + 1) % 2)
                    if not last_it:
                        for c in SPLIT_AT.get(j, []):
                            split((NCH + OWN * it + 2 + c) // 2 + 1, c % 2, (s_chunk, NCH * (2 * it + 1) + c + 1), flat(w_hi, c))
                    if not (last_it and j >= TPB - 2):
                        copy_current(tile + 2, j)
                    chunk(0, 1)
                    chunk(1, 1)
                    chunk(2, 0)
                    if j == 2:
                        high_x(TPB + it, 1 - it // KV_HEADS, (it % KV_HEADS) * P, bank_vt)

            root(0)
            for c in range(2):
                split(c // 2 + 1, c % 2, (s_chunk, 0), flat(w_hi, c))
            for t in range(TPK):
                high_x(t, 0, t * P, banks[t % 4])
            split(2, 0, (s_chunk, 0), flat(w_hi, 2))
            root(1)
            split(2, 1, (s_chunk, 0), flat(w_hi, 3))
            swap(0, 0, 0)
            for t in (TPK, TPK + 1):
                high_x(t, 0, t * P, banks[t % 4])
            high(0, 0, 0)
            swap(0, 0, 1)
            for t in (TPK + 2, TPK + 3):
                high_x(t, 0, t * P, banks[t % 4])
            for c in range(4, NCH):
                split(c // 2 + 1, c % 2, (s_chunk, 0), flat(w_hi, c))
            high(0, 0, 1)
            for c in range(2, QK):
                swap(0, 0, c)
                if c > 2:
                    high(0, 0, c - 1)
            copy_v(0)
            high(0, 0, QK - 1)
            root(2, TPB)
            swap(1, 1, 0)
            copy_current(0, 0)
            exponential(0, 0)
            high(1, 1, 0)
            place_v(0, 0)
            copy_current(1, 1)
            swap(1, 1, 1)
            loops(act, body)

        @block.vector
        def _(dve):
            dve.memset(neg[:, :], NEG).then_inc(s_neg, 1)
            dve.wait_ge(s_masks, 16)

            def rotate_a(block, par, c):
                r, slot = QK * block + c, (par + c) % 2
                dve.wait_ge(s_swap, 2 * (r + 1))
                wait(dve, s_qklo, r - 1)
                dve.tensor_tensor(rot_a[:, slot, :], bank_chunk[c % 2][:, :], cos_sin[:, 0, par * BLK:(par + 1) * BLK],
                                  ALU.mult).then_inc(s_rot_a, 1)

            def rotate(block, par, c):
                r, slot = QK * block + c, (par + c) % 2
                dve.wait_ge(s_rot_b, r + 1)
                dve.wait_ge(s_rot_a, r + 1)
                dve.tensor_tensor(rot_a[:, slot, :], rot_a[:, slot, :], rot_b[:, slot, :], ALU.add).then_inc(s_rot, 1)

            def merge(tile, j):
                cur = prob[:, j % 2, :, :]
                copied = 2 * (tile + 1) if isinstance(tile, int) else dve.to_reg(2 * (tile + 1))
                dve.wait_ge(s_neg, 1)
                dve.wait_ge(s_cur, copied)
                for b in range(2):
                    mask = after_t.bitcast(U32).unsqueeze(1).to_broadcast([P, 2, P])
                    if j % TPB == 0:
                        src = neg[:, :].unsqueeze(1).to_broadcast([P, 2, P])
                    else:
                        src = bank_s[b][:, :].rearrange("p (h s n) -> p h s n", h=2, s=2)[:, :, 0, :]
                    last = dve.copy_predicated(prob[:, j % 2, 2 * b:2 * b + 2, :], mask, src)
                last.then_inc(s_merged, 1)
                dve.wait_ge(s_merged, tile + 1)
                wait(dve, s_pexp, tile - 1)
                dve.tensor_reduce(negmax[:, j % 2, :], cur, AX.X, ALU.max, negate=True).then_inc(s_negmax, 1)

            def invert(tile, j):
                dve.wait_ge(s_pexp, tile + 1)
                wait(dve, s_prob, tile - 1)
                dve.reciprocal(rinv[:, j % 2, :], rowsum[:, j % 2, :]).then_inc(s_rinv, 1)

            steps = [0]

            def link(ins):
                steps[0] += 1
                ins.then_inc(s_step, 1)
                dve.wait_ge(s_step, steps[0])

            def moments(tiles):
                for n in tiles:
                    if n < TPK:
                        dve.wait_ge(s_row[n], 16)
                    else:
                        dve.wait_ge(s_rows[n // TPK], 16)
                    dve.bn_stats(stats[:, n % TPB, :], x_rows[n // TPB][:, n % TPB, :]).then_inc(s_bn, 1)

            def statistics(tiles, g):
                dve.wait_ge(s_bn, tiles[-1] + 1)
                for n in tiles:
                    last = dve.bn_aggr(mv[:, n, :], stats[:, n % TPB, :])
                link(last)
                at, n = slice(tiles[0], tiles[-1] + 1), len(tiles)
                var, root, t = (rs[:, i, 0:n] for i in range(3))
                dve.tensor_scalar(var, mv[:, at, 1], EPS, None, ALU.add).then_inc(s_var, 1)
                dve.wait_ge(s_root, g + 1)
                r = rstd[:, at]
                link(dve.reciprocal(r, root))
                link(dve.tensor_tensor(t, r, r, ALU.mult))
                link(dve.tensor_tensor(t, t, var, ALU.mult))
                link(dve.tensor_scalar(t, t, -0.5, 1.5, ALU.mult, ALU.add))
                link(dve.tensor_tensor(r, r, t, ALU.mult))

            def normalise_x(t, rows):
                def column(a):
                    return a[:, t:t + 1] if isinstance(t, int) else a[:, bass.ds(t, 1)]

                mean = mv[:, t, 0:1] if isinstance(t, int) else mv[:, bass.ds(t, 1), 0]
                dve.tensor_scalar(rows, rows, mean, column(rstd), ALU.subtract, ALU.mult).then_inc(s_xn, 1)

            def low_x(n, batch, tok, bank):
                dve.wait_ge(s_xhi, n + 1)
                if isinstance(batch, int) and isinstance(tok, int):
                    hi, lo = (a[:, batch, :, tok:tok + P] for a in (xn_hi, xn_lo))
                else:
                    hi, lo = (a[:, bass.ds(batch, 1), :, bass.ds(tok, P)].rearrange("p a k n -> p (a k) n")
                              for a in (xn_hi, xn_lo))
                dve.tensor_tensor(lo, bank[:, :].rearrange("p (k n) -> p k n", k=KT), hi.bitcast(F32),
                                  ALU.subtract).then_inc(s_xlo, 1)

            def scale_x(it, t, base):
                count = [0]

                def link_tile(ins):
                    count[0] += 1
                    ins.then_inc(s_step, 1)
                    dve.wait_ge(s_step, base + SCALE_STEPS * it + count[0])

                b = beta[:, t:t + 1] if isinstance(t, int) else beta[:, bass.ds(t, 1)]
                dve.wait_ge(s_abs, it + 1)
                link_tile(dve.tensor_scalar(xk[:, :], abs_sum[:, :], 1.0 / HID, EPS, ALU.mult, ALU.add))
                dve.tensor_scalar(b, abs_sum[:, :], 1.0 / HID, None, ALU.mult)
                link_tile(dve.reciprocal(xk[:, :], xk[:, :]))
                link_tile(dve.tensor_scalar(xk[:, :], xk[:, :], SQRT7, None, ALU.mult))
                dve.wait_ge(s_xtr, TPB + it + 1)
                dve.tensor_scalar(xt[:, :], xt[:, :], xk[:, :], MAGIC, ALU.mult, ALU.add).then_inc(s_vq, 1)

            SCALE_STEPS = 3

            def low_v(block, par):
                dve.wait_ge(s_v, block + 1)
                tiles = slice(par * TPK, (par + 1) * TPK)
                dve.tensor_tensor(v_lo[:, tiles, :], bank_vt[:, :].rearrange("p (t n) -> p t n", n=HD),
                                  v_hi[:, tiles, :].bitcast(F32), ALU.subtract).then_inc(s_vlo, 1)

            def accumulate(it, j, fresh):
                tile = TPB * it + j
                dve.wait_ge(s_wo, tile + 1)
                if fresh:
                    wait(dve, s_store[j], 16 * (it // KV_HEADS))
                    dve.tensor_copy(acc[:, j, :], bank_wo[:, :]).then_inc(s_acc, 1)
                else:
                    dve.wait_ge(s_acc, tile - TPB + 1)
                    dve.tensor_tensor(acc[:, j, :], bank_wo[:, :], acc[:, j, :], ALU.add).then_inc(s_acc, 1)

            def low_o(tile):
                dve.wait_ge(s_ohi, tile + 1)
                wait(dve, s_wo, tile)
                dve.tensor_tensor(o_lo[:, :, :], heads(bank_pv[:, :]), o_hi[:, :, :].bitcast(F32),
                                  ALU.subtract).then_inc(s_olo, 1)

            def body(it, last_it, fresh=False):
                t_x = (1 - it // KV_HEADS) * TPB + it % KV_HEADS
                for j in range(TPB):
                    tile, s = TPB * it + j, j % TPK
                    block = 2 * it + j // TPK

                    def chunk(place, step):
                        if finished(s, place) is None or (j == 0 and step == 1):
                            return
                        ahead, c = finished(s, place)
                        nxt = j // TPK + ahead
                        if c == V or (nxt >= 2 and last_it):
                            return
                        (rotate_a, rotate)[step](block + ahead, nxt % 2, c)

                    dve.wait_ge(s_ptr, tile + 1)
                    wait(dve, s_pv, tile)
                    dve.tensor_tensor(pt[:, 0, :, :], heads(bank_pt[:, :]), over_heads(on_or_before), ALU.mult).then_inc(s_ptc, 1)
                    if j > 0:
                        dve.tensor_tensor(pt[:, 1, :, :], heads(bank_pt[:, :]), over_heads(after), ALU.mult).then_inc(s_ptp, 1)
                    if late(it, j, last_it) and j != 1:
                        rotate_a(*late(it, j, last_it))
                    for before, (high, low) in enumerate(((s_pch, s_pcl), (s_pph, s_ppl))[:min(j, 1) + 1]):
                        if before == 1 and s == 2:
                            continue
                        wait(dve, high, tile + 1 if before == 0 else (TPB - 1) * it + j)
                        dve.tensor_tensor(pt_lo[:, before, :, :], pt[:, before, :, :],
                                          pt_hi[:, before, :, :].bitcast(F32), ALU.subtract).then_inc(low, 1)
                    if late(it, j, last_it):
                        rotate(*late(it, j, last_it))
                    if j > 0:
                        accumulate(it, j - 1, fresh)
                    if last_it and j == TPK + 1:
                        dve.wait_ge(s_chunk, NCH * 2 * ITERS)
                        weights.pad(dve)
                    if j == 1:
                        dve.wait_ge(s_xt, 16 * (it + 1) if isinstance(it, int) else (it + 1) * 16)
                        normalise_x(t_x, xt[:, :])
                    if not (last_it and j == TPB - 1):
                        invert(tile + 1, j + 1)
                    if j == 0:
                        low_o(tile)
                        for h in range(2, GROUP):
                            dve.wait_ge(s_whi, NCH + PIECES * it + h + 1)
                            dve.tensor_tensor(wo_lo[:, h, :], raw[:, h, :], wo_hi[:, h, :].bitcast(F32),
                                              ALU.subtract).then_inc(s_wlo2, 1)
                    chunk(0, 0)
                    chunk(1, 0)
                    if last_it and j == TPB - 1:
                        weights.sum_abs_dve(dve, 1, 0)
                    if j > 0:
                        low_o(tile)
                    if s == 3 and not (last_it and j == TPB - 1):
                        low_v(block + 1, (j // TPK + 1) % 2)
                    if j != 1:
                        chunk(0, 1)
                        chunk(1, 1)
                    if not (last_it and j >= TPB - 2):
                        merge(tile + 2, j + 2)
                    if j == 1:
                        chunk(0, 1)
                        chunk(1, 1)
                    if j == 2:
                        scale_x(it, t_x, steps[0])
                        low_x(TPB + it, 1 - it // KV_HEADS, (it % KV_HEADS) * P, bank_vt)
                    if last_it and j == TPB - 1:
                        weights.scales(dve, 0, bank_chunk[0])
                        for i in (1, 2):
                            weights.sum_abs_dve(dve, 1, i)
                accumulate(it, TPB - 1, fresh)

            for g in range(TPB // TPK):
                tiles = range(TPK * g, TPK * (g + 1))
                moments(tiles)
                statistics(tiles, g)
                for t in tiles:
                    normalise_x(t, x_rows[0][:, t, :])
                if g == 0:
                    for t in tiles:
                        low_x(t, 0, t * P, banks[t % 4])
            dve.wait_ge(s_rope, 16)
            for c in range(2):
                rotate_a(0, 0, c)
                for t in (TPK + 2 * c, TPK + 2 * c + 1):
                    low_x(t, 0, t * P, banks[t % 4])
                rotate(0, 0, c)
            second = range(TPB, TILES)
            for c in range(2, QK):
                rotate_a(0, 0, c)
                if c > 2:
                    rotate(0, 0, c - 1)
                moments(second[2 * (c - 2):2 * (c - 1)])
            rotate(0, 0, QK - 1)
            moments(second[2 * (QK - 2):])
            statistics(second, 2)
            rotate_a(1, 1, 0)
            merge(0, 0)
            invert(0, 0)
            rotate(1, 1, 0)
            low_v(0, 0)
            merge(1, 1)
            body(0, False, fresh=True)
            with dve.Fori(1, KV_HEADS) as it:
                body(it, False)
            body(KV_HEADS, False, fresh=True)
            with dve.Fori(KV_HEADS + 1, ITERS - 1) as it:
                body(it, False)
            body(ITERS - 1, True)

        @block.gpsimd
        def _(pool):
            def rotate_b(block, par, c):
                r, slot = QK * block + c, (par + c) % 2
                pool.wait_ge(s_swap, 2 * (r + 1))
                pool.tensor_tensor(rot_b[:, slot, :], rot_b[:, slot, :], cos_sin[:, 1, par * BLK:(par + 1) * BLK],
                                   ALU.mult).then_inc(s_rot_b, 1)

            def low(block, par, c):
                r, slot = QK * block + c, (par + c) % 2
                pool.wait_ge(s_qkhi, r + 1)
                if c == 0:
                    hi, lo = (t[:, par * BLK:(par + 1) * BLK] for t in (k_hi, k_lo))
                else:
                    hi, lo = (q_block(t, c - 1, par) for t in (q_hi, q_lo))
                src = rot_a[:, slot, :]
                if c > 0:
                    src = src.rearrange("p (a n) -> p a n", a=2)
                pool.tensor_tensor(lo, src, hi.bitcast(F32), ALU.subtract).then_inc(s_qklo, 1)

            def split(count, ring, hi, lo):
                pool.wait_ge(s_whi, count + 1)
                pool.tensor_tensor(lo, raw[:, ring, :], hi.bitcast(F32), ALU.subtract).then_inc(s_wlo, 1)

            def normalise(tile, j):
                pool.wait_ge(s_rinv, tile + 1)
                cur = prob[:, j % 2, :, :]
                pool.tensor_tensor(cur, cur, over_keys(rinv[:, j % 2, :]), ALU.mult).then_inc(s_prob, 1)

            def flat(w, c):
                return w[:, c, :, :].rearrange("p k n -> p (k n)")

            def body(it, last_it):
                for j in range(TPB):
                    tile, s = TPB * it + j, j % TPK
                    block = 2 * it + j // TPK

                    def chunk(place, step):
                        if finished(s, place) is None or (j == 0 and step == 1):
                            return
                        ahead, c = finished(s, place)
                        nxt = j // TPK + ahead
                        if c == V or (nxt >= 2 and last_it):
                            return
                        (rotate_b, low)[step](block + ahead, nxt % 2, c)

                    if j == 0:
                        normalise(tile + 1, j + 1)
                        split(NCH + PIECES * it, 0, wo_hi[:, 0, :], wo_lo[:, 0, :])
                        split(NCH + PIECES * it + 1, 1, wo_hi[:, 1, :], wo_lo[:, 1, :])
                    if s == 2:
                        pool.wait_ge(s_pph, (TPB - 1) * it + j)
                        pool.tensor_tensor(pt_lo[:, 1, :, :], pt[:, 1, :, :], pt_hi[:, 1, :, :].bitcast(F32),
                                           ALU.subtract).then_inc(s_ppl, 1)
                    if late(it, j, last_it):
                        low(*late(it, j, last_it))
                    if j > 0 and not (last_it and j == TPB - 1):
                        normalise(tile + 1, j + 1)
                    chunk(0, 0)
                    chunk(1, 0)
                    pieces = [] if last_it else SPLIT_AT.get(j, [])
                    for c in pieces[:1]:
                        split(NCH + PIECES * it + GROUP + c, c % 2, flat(w_hi, c), flat(w_lo, c))
                    chunk(0, 1)
                    chunk(1, 1)
                    for c in pieces[1:]:
                        split(NCH + PIECES * it + GROUP + c, c % 2, flat(w_hi, c), flat(w_lo, c))
                    chunk(2, 0)

            pool.wait_ge(s_rope, 16)
            for c in range(4):
                split(c, c % 2, flat(w_hi, c), flat(w_lo, c))
            rotate_b(0, 0, 0)
            low(0, 0, 0)
            rotate_b(0, 0, 1)
            for c in range(4, NCH):
                split(c, c % 2, flat(w_hi, c), flat(w_lo, c))
            low(0, 0, 1)
            for c in range(2, QK):
                rotate_b(0, 0, c)
                if c > 2:
                    low(0, 0, c - 1)
            low(0, 0, QK - 1)
            rotate_b(1, 1, 0)
            normalise(0, 0)
            low(1, 1, 0)
            rotate_b(1, 1, 1)
            loops(pool, body)
            weights.round(pool, 0)


def ffn(nc, arena, banks, x, const, beta, weights, s_store, q4_dram, s_dram, out):
    sem = nc.alloc_semaphore
    ident = const[:, 0, :]
    w_t = [arena.tensor(f"w_t{m}", [P, KT, IPAD], BF16) for m in range(2)]
    wd_t = arena.tensor("wd_t", [P, IT, HID], BF16)
    ident_bf = arena.tensor("ident_bf", [P, P], BF16)
    c_gate = arena.tensor("c_gate", [P, TILES], F32)
    c_up = arena.tensor("c_up", [P, TILES], F32)
    tile_gate = arena.tensor("tile_gate", [P, 2], F32)
    q4 = arena.tensor("q4", [P, 2, HID], BF16)
    xq_t = arena.tensor("xq_t", [P, 2, HID], BF16)
    relu = arena.tensor("relu", [P, NC, 512], F32)
    inter = arena.tensor("inter", [P, 2, IPAD], F32)
    q8_t = arena.tensor("q8_t", [P, 2, IT, P], BF16)
    maxima = arena.tensor("maxima", [P, 2, 2], F32)
    gamma = arena.tensor("gamma", [P, 2], F32)
    gk = arena.tensor("gk", [P, 2], F32)
    c_half = arena.tensor("c_half", [P, 2], F32)
    th = arena.tensor("th", [P, HID], F32)
    gout = arena.tensor("gout", [P, 2, HID], F32)
    x_in = arena.tensor("x_in", [P, 2, HID], F32)
    att_in = arena.tensor("att_in", [P, 2, HID], F32)

    s_ident, s_wtr, s_clip, s_cgu = (sem(n) for n in ("s_ident", "s_wtr", "s_clip", "s_cgu"))
    s_wt = [sem("s_wt_act"), sem("s_wt_dve")]
    s_link = sem("s_link")
    s_q4in = [sem(f"s_q4in{r}") for r in range(2)]
    s_fin = [sem(f"s_fin{r}") for r in range(2)]
    s_out = [sem(f"s_out{r}") for r in range(2)]
    s_tx, s_xq, s_tgate, s_gu, s_relu, s_ug, s_inter = (
        sem(n) for n in ("s_tx", "s_xq", "s_tgate", "s_gu", "s_relu", "s_ug", "s_inter"))
    s_v8, s_t8, s_q8t, s_down, s_chalf, s_th, s_th1, s_g, s_mul, s_res = (
        sem(n) for n in ("s_v8", "s_t8", "s_q8t", "s_down", "s_chalf", "s_th", "s_th1", "s_g", "s_mul", "s_res"))

    W_TR = [(m, i) for m in range(3) for i in range(IT)]
    DOWN = 2 * IT
    T8 = [(0, 4), (4, 8), (8, IT)]

    def weight_bank(k):
        return banks[k % 4] if k < DOWN else banks[4 + k % 3]

    def weight_dst(k):
        m, i = W_TR[k]
        return w_t[m][:, :, i * P:(i + 1) * P] if m < 2 else wd_t[:, i, :]

    def weight_src(k):
        b = weight_bank(k)[:, :]
        return b.rearrange("p (k n) -> p k n", k=KT) if k < DOWN else b

    def taken(eng, k):
        wait(eng, s_wt[k % 2], k // 2 + 1)

    def column(a, t):
        return a[:, t:t + 1] if isinstance(t, int) else a[:, bass.ds(t, 1)]

    def tile_rows(dram, t):
        return dram[t * P:(t + 1) * P, :] if isinstance(t, int) else dram[bass.ds(t * P, P), :]

    def steps(eng, step):
        step(0, 0)
        step(1, 1)
        with eng.Fori(1, TILES // 2 - 2) as i:
            for ring in range(2):
                step(2 * i + ring, ring)
        step(TILES - 4, 0)
        step(TILES - 3, 1)

    with nc.Block() as block:
        @block.sync
        def _(sp):
            x_flat, out_flat = (a.rearrange("b t n -> (b t) n") for a in (x, out))

            def load_q4(t, ring):
                if not isinstance(t, int) or t >= 2:
                    sp.wait_ge(s_tx, t - 1)
                sp.dma_start(q4[:, ring, :], tile_rows(q4_dram, t)).then_inc(s_q4in[ring], 16)

            def load_rest(t, ring):
                sp.dma_start(x_in[:, ring, :], tile_rows(x_flat, t)).then_inc(s_fin[ring], 16)
                sp.dma_start(att_in[:, ring, :], tile_rows(s_dram, t)).then_inc(s_fin[ring], 16)

            for t in range(2):
                load_q4(t, t)
            for s in s_store:
                sp.wait_ge(s, 32)
            for t in range(2):
                load_rest(t, t)
            for t in range(2, 4):
                load_q4(t, t % 2)

            def step(t, ring):
                if not isinstance(t, int) or t + 4 < TILES:
                    load_q4(t + 4, ring)
                sp.wait_ge(s_res, t + 1)
                sp.dma_start(tile_rows(out_flat, t), gout[:, ring, :]).then_inc(s_out[ring], 16)
                if not isinstance(t, int) or t + 2 < TILES:
                    load_rest(t + 2, ring)

            steps(sp, step)
            step(TILES - 2, 0)
            step(TILES - 1, 1)
            for ring in range(2):
                sp.wait_ge(s_out[ring], 16 * (TILES // 2))

        @block.gpsimd
        def _(pool):
            for m in (1, 2):
                weights.round(pool, m)

            def combine(t, ring, chunks):
                for c in chunks:
                    at, n = CHUNKS[c]
                    pool.wait_ge(s_ug, NC * t + c + 1)
                    part = inter[:, ring, at:at + n]
                    pool.tensor_tensor(part, part, relu[:, c, 0:n], ALU.mult).then_inc(s_inter, 1)

            def result(t, ring):
                pool.wait_ge(s_g, t + 1)
                pool.wait_ge(s_fin[ring], 32 * (t // 2 + 1) if isinstance(t, int) else (t // 2 + 1) * 32)
                g = gout[:, ring, :]
                pool.tensor_tensor(g, g, att_in[:, ring, :], ALU.mult).then_inc(s_mul, 1)
                pool.wait_ge(s_mul, t + 1)
                pool.tensor_tensor(g, g, x_in[:, ring, :], ALU.add).then_inc(s_res, 1)

            combine(0, 0, range(NC))
            combine(1, 1, range(NC))

            def step(t, ring):
                combine(t + 2, ring, range(NC))
                result(t, ring)

            steps(pool, step)
            result(TILES - 2, 0)
            result(TILES - 1, 1)

        @block.scalar
        def _(act):
            def take(ks):
                for k in ks:
                    if k % 2 == 0:
                        act.wait_ge(s_wtr, k + 1)
                        act.activation(weight_dst(k), weight_src(k), ACT.Copy, bias=-MAGIC).then_inc(s_wt[0], 1)

            def gate_scale(t, ring):
                act.wait_ge(s_cgu, 1)
                act.activation(tile_gate[:, ring:ring + 1], column(c_gate, t), ACT.Copy).then_inc(s_tgate, 1)
                act.wait_ge(s_tgate, t + 1)

            def gate(t, ring, c):
                k, n = NC * t + c, CHUNKS[c][1]
                act.wait_ge(s_gu, k + 1)
                wait(act, s_inter, k - 2)
                act.activation(relu[:, c, 0:n], banks[(NC * ring + c) % 2][:, 0:n], ACT.Relu,
                               scale=tile_gate[:, ring:ring + 1]).then_inc(s_relu, 1)

            def quantised(t, ring):
                wait(act, s_down, t - 1)
                for p, (a, b) in enumerate(T8):
                    act.wait_ge(s_t8, 3 * t + p + 1)
                    act.activation(q8_t[:, ring, a:b, :].rearrange("p i n -> p (i n)"),
                                   banks[4 + (3 * ring + p) % 2][:, 0:(b - a) * P], ACT.Copy, bias=-MAGIC).then_inc(s_q8t, 1)

            def tanh(t, ring):
                act.wait_ge(s_down, t + 1)
                act.wait_ge(s_chalf, t + 1)
                wait(act, s_g, t)
                act.activation(th[:, :], banks[6][:, :], ACT.Tanh, scale=c_half[:, ring:ring + 1]).then_inc(s_th, 1)

            take(range(DOWN))
            for t in range(2):
                gate_scale(t, t)
                for c in range(NC):
                    gate(t, t, c)
            take(range(DOWN, len(W_TR)))
            quantised(0, 0)

            def step(t, ring):
                tanh(t, ring)
                gate_scale(t + 2, ring)
                gate(t + 2, ring, 0)
                gate(t + 2, ring, 1)
                quantised(t + 1, 1 - ring)
                gate(t + 2, ring, 2)

            steps(act, step)
            tanh(TILES - 2, 0)
            quantised(TILES - 1, 1)
            tanh(TILES - 1, 1)

        @block.vector
        def _(dve):
            count = [0]

            def link(ins):
                count[0] += 1
                ins.then_inc(s_link, 1)
                dve.wait_ge(s_link, count[0])

            dve.tensor_copy(ident_bf[:, :], ident).then_inc(s_ident, 1)

            def take(ks):
                for k in ks:
                    if k % 2 == 1:
                        dve.wait_ge(s_wtr, k + 1)
                        dve.tensor_scalar(weight_dst(k), weight_src(k), -MAGIC, None, ALU.add).then_inc(s_wt[1], 1)

            def clip(m, chunks=CHUNKS):
                taken(dve, IT * (m + 1) - 1)
                taken(dve, IT * (m + 1) - 2)
                for w in [w_t[m][:, :, at:at + n] for at, n in chunks] if m < 2 else [wd_t[:, :, :]]:
                    dve.tensor_scalar(w, w, 1.0, -1.0, ALU.min, ALU.max).then_inc(s_clip, 1)

            weights.sum_abs_dve(dve, 1, 3)
            take(range(4))
            weights.scales(dve, 1, banks[6])
            weights.scales(dve, 2, banks[5])
            take(range(4, IT))
            take(range(IT, IT + 4))
            clip(0)
            for s in s_store:
                dve.wait_ge(s, 32)
            dve.tensor_scalar(c_up[:, :], beta[:, :], weights.scale[:, 1:2], None, ALU.mult)
            dve.tensor_scalar(c_gate[:, :], beta[:, :], weights.scale[:, 0:1], None, ALU.mult).then_inc(s_cgu, 1)
            dve.wait_ge(s_cgu, 1)
            take(range(IT + 4, DOWN))
            def clip_x(t, ring):
                dve.wait_ge(s_tx, t + 1)
                wait(dve, s_gu, NC * (t - 1))
                dve.tensor_scalar(xq_t[:, ring, :], banks[7][:, 0:HID // 2].bitcast(BF16), 7.0, -8.0,
                                  ALU.min, ALU.max).then_inc(s_xq, 1)

            def up_gate(t, ring, c):
                at, n = CHUNKS[c]
                dve.wait_ge(s_relu, NC * t + c + 1)
                wait(dve, s_t8, len(T8) * (t - 1))
                dve.scalar_tensor_tensor(inter[:, ring, at:at + n], banks[2 + (NC * ring + c) % 2][:, 0:n],
                                         column(c_up, t), relu[:, c, 0:n], ALU.mult, ALU.mult).then_inc(s_ug, 1)

            base = count[0]
            SMALL = 5

            def scales(t, ring):
                done = [0]

                def link_tile(ins):
                    done[0] += 1
                    ins.then_inc(s_link, 1)
                    dve.wait_ge(s_link, base + SMALL * t + done[0])

                g, r = gamma[:, ring:ring + 1], gk[:, ring:ring + 1]
                for i, (a, b) in enumerate(((0, CHUNKS[2][0]), (CHUNKS[2][0], IPAD))):
                    dve.wait_ge(s_inter, NC * t + 2 + i)
                    last = dve.tensor_reduce(maxima[:, ring, i:i + 1], inter[:, ring, a:b], AX.X, ALU.max,
                                             apply_absolute_value=True)
                link_tile(last)
                link_tile(dve.tensor_reduce(g, maxima[:, ring, :], AX.X, ALU.max))
                link_tile(dve.tensor_scalar(r, g, EPS, None, ALU.add))
                link_tile(dve.reciprocal(r, r))
                link_tile(dve.tensor_scalar(r, r, 127.0, None, ALU.mult))
                dve.tensor_scalar(inter[:, ring, :], inter[:, ring, :], r, MAGIC, ALU.mult, ALU.add).then_inc(s_v8, 1)
                wait(dve, s_g, t - 1)
                dve.tensor_scalar(c_half[:, ring:ring + 1], g, 0.5 / 127.0, weights.scale[:, 2:3],
                                  ALU.mult, ALU.mult).then_inc(s_chalf, 1)
                assert done[0] == SMALL

            def silu(t, ring):
                dve.wait_ge(s_th, t + 1)
                dve.tensor_scalar(th[:, :], th[:, :], 1.0, None, ALU.add).then_inc(s_th1, 1)
                dve.wait_ge(s_th1, t + 1)
                wait(dve, s_out[ring], 16 * (t // 2))
                dve.scalar_tensor_tensor(gout[:, ring, :], banks[6][:, :], c_half[:, ring:ring + 1], th[:, :],
                                         ALU.mult, ALU.mult).then_inc(s_g, 1)

            clip(1, CHUNKS[:1])
            clip_x(0, 0)
            clip_x(1, 1)
            clip(1, CHUNKS[1:])
            for c in range(NC):
                up_gate(0, 0, c)
            clip_x(2, 0)
            up_gate(1, 1, 0)
            scales(0, 0)
            up_gate(1, 1, 1)
            up_gate(1, 1, 2)
            take(range(DOWN, len(W_TR)))
            clip(2)
            scales(1, 1)

            def step(t, ring):
                up_gate(t + 2, ring, 0)
                silu(t, ring)
                up_gate(t + 2, ring, 1)
                up_gate(t + 2, ring, 2)
                if not isinstance(t, int) or t + 3 < TILES:
                    clip_x(t + 3, 1 - ring)
                scales(t + 2, ring)

            steps(dve, step)
            silu(TILES - 2, 0)
            silu(TILES - 1, 1)

        @block.tensor
        def _(pe):
            def transpose_weights(k):
                m, i = W_TR[k]
                pe.wait_ge(weights.s_wscaled[m], 1 if m < 2 and (i + 1) * HID <= ROUND_PARTS[0][1] else 2)
                if k < DOWN and k >= 4:
                    taken(pe, k - 4)
                if k >= DOWN + 3:
                    taken(pe, k - 3)
                for q in range(KT):
                    at = i * HID + q * P if m < 2 else q * IPAD + i * P
                    last = pe.transpose(weight_bank(k)[:, q * P:(q + 1) * P], weights.raw[m][:, at:at + P], ident)
                last.then_inc(s_wtr, 1)

            def transpose_x(t, ring):
                pe.wait_ge(s_q4in[ring], 16 * (t // 2 + 1) if isinstance(t, int) else (t // 2 + 1) * 16)
                wait(pe, s_xq, t)
                for q in range(KT):
                    last = pe.transpose(banks[7][:, 0:HID // 2].bitcast(BF16)[:, q * P:(q + 1) * P],
                                        q4[:, ring, q * P:(q + 1) * P], ident_bf[:, :])
                last.then_inc(s_tx, 1)

            def gate_up(t, ring, c, products=(0, 1)):
                at, n = CHUNKS[c]
                k, slot = NC * t + c, (NC * ring + c) % 2
                pe.wait_ge(s_xq, t + 1)
                wait(pe, s_relu, k - 1)
                wait(pe, s_ug, k - 1)
                for m in products:
                    for q in range(KT):
                        last = pe.matmul(banks[2 * m + slot][:, 0:n], xq_t[:, ring, q * P:(q + 1) * P],
                                         w_t[m][:, q, at:at + n], start=(q == 0), stop=(q == KT - 1))
                if 1 in products:
                    last.then_inc(s_gu, 1)

            def transpose_8(t, ring, pieces=range(len(T8))):
                pe.wait_ge(s_v8, t + 1)
                for p in pieces:
                    a, b = T8[p]
                    wait(pe, s_q8t, 3 * t + p - 1)
                    for i in range(a, b):
                        last = pe.transpose(banks[4 + (3 * ring + p) % 2][:, (i - a) * P:(i - a + 1) * P],
                                            inter[:, ring, i * P:(i + 1) * P], ident)
                    last.then_inc(s_t8, 1)

            def down(t, ring):
                pe.wait_ge(s_q8t, len(T8) * (t + 1))
                wait(pe, s_g, t)
                for i in range(IT):
                    last = pe.matmul(banks[6][:, :], q8_t[:, ring, i, :], wd_t[:, i, :],
                                     start=(i == 0), stop=(i == IT - 1))
                last.then_inc(s_down, 1)

            pe.wait_ge(s_ident, 1)
            for k in range(4):
                transpose_weights(k)
            weights.total(pe, 1, banks[6])
            weights.total(pe, 2, banks[5])
            for k in range(4, DOWN):
                transpose_weights(k)
            transpose_x(0, 0)
            transpose_x(1, 1)
            for c in range(NC):
                pe.wait_ge(s_clip, NC + c + 1)
                gate_up(0, 0, c)
            transpose_x(2, 0)
            for c in range(NC):
                gate_up(1, 1, c)
            pe.wait_ge(weights.s_winv, 3)
            for k in range(DOWN, len(W_TR)):
                transpose_weights(k)
            taken(pe, len(W_TR) - 1)
            taken(pe, len(W_TR) - 2)
            transpose_8(0, 0)
            pe.wait_ge(s_clip, 2 * NC + 1)
            down(0, 0)

            def step(t, ring):
                gate_up(t + 2, ring, 0)
                gate_up(t + 2, ring, 1)
                transpose_8(t + 1, 1 - ring, (0, 1))
                gate_up(t + 2, ring, 2, (0,))
                transpose_8(t + 1, 1 - ring, (2,))
                gate_up(t + 2, ring, 2, (1,))
                if not isinstance(t, int) or t + 3 < TILES:
                    transpose_x(t + 3, 1 - ring)
                down(t + 1, 1 - ring)

            steps(pe, step)
            transpose_8(TILES - 1, 1)
            down(TILES - 1, 1)


_INS = ['L0_attn_x', 'L0_attn_wq', 'L0_attn_wk', 'L0_attn_wv', 'L0_attn_wo', 'L0_ffn_w_gate', 'L0_ffn_w_up',
        'L0_ffn_w_down', 'L0_ffn_s_gate', 'L0_ffn_s_up', 'L0_ffn_s_down']


def kernel(**inputs):
    import numpy as _np
    import concourse.bacc as _bacc
    from concourse import mybir as _mybir
    from concourse.bass_utils import run_bass_kernel_spmd as _run

    half = HD // 2
    inv_freq = (_np.float32(10000.0) ** (-_np.arange(half, dtype=_np.float32) / _np.float32(half))).astype(_np.float32)
    ang = _np.arange(SEQ, dtype=_np.float32)[None, :] * inv_freq[:, None]
    cos, sin = (f(ang.astype(_np.float64)) * HD**-0.25 for f in (_np.cos, _np.sin))
    rope = _np.stack([_np.concatenate([cos, cos]), _np.concatenate([-sin, sin])], axis=1).astype(_np.float32)
    one = _np.ones((P, P), _np.float32)
    masks = _np.stack([_np.eye(P, dtype=_np.float32), _np.triu(one), _np.tril(one, -1), _np.triu(one, 1)], axis=1)

    nc = _bacc.Bacc("TRN2", target_bir_lowering=False, num_devices=1)
    arrays, args = {}, []
    for name, a in [(n, inputs[n]) for n in _INS] + [("rope", rope), ("masks", masks)]:
        a = _np.ascontiguousarray(a)
        arrays[f"in_{name}_dram"] = a
        args.append(nc.dram_tensor(f"in_{name}_dram", a.shape, _mybir.dt.from_np(a.dtype), kind="ExternalInput").ap())
    shape = (BATCH, SEQ, HID)
    args.append(nc.dram_tensor("out_0_dram", shape, _mybir.dt.float32, kind="ExternalOutput").ap())
    build_kernel(nc, *args)
    r = _run(nc, [arrays], core_ids=[0])
    return r.results[0]["out_0_dram"]
```
